# Optimizing a Trainium2 kernel written in Bass

```python
import numpy as np
import jax
import jax.numpy as jnp

def _softmax(x, axis=-1):
    return jax.nn.softmax(x, axis=axis)

def _gelu(x):
    return jax.nn.gelu(x, approximate=True)

def _silu(x):
    return jax.nn.silu(x)

def _sigmoid(x):
    return jax.nn.sigmoid(x)

def _layernorm(x, axis=-1, eps=1e-05):
    m = jnp.mean(x, axis=axis, keepdims=True)
    v = jnp.var(x, axis=axis, keepdims=True)
    return (x - m) / jnp.sqrt(v + eps)

def _scatter_add(tgt, idx, src, axis=0):
    return tgt.at[idx].add(src)

def _segment_sum(src, seg, n):
    return jax.ops.segment_sum(src, seg, n)
kernel_name = 'mk_adj_preln_d1_adj_r2_e38114'

def setup_inputs(seed: int=0):
    np.random.seed(seed)
    _w = jnp.asarray

    def _rec_inputs():
        import jax
        import jax.numpy as jnp
        _gk = jax.random.key(seed)
        x = -0.000929 + 1 * jax.random.normal(jax.random.fold_in(_gk, 1), (8192, 128), jnp.float32)
        _w = (1.0 + jnp.arange(8192, dtype=jnp.float32)) ** (-0.5)
        _w = _w / _w.mean()
        _pij = jnp.clip(0.00195312 * _w[:, None] * _w[None, :], 0.0, 1.0)
        _a = jax.random.uniform(jax.random.fold_in(_gk, 2), (8192, 8192)) < _pij
        _a = jnp.logical_or(_a, jnp.eye(8192, dtype=bool))
        _af = _a.astype(jnp.float32)
        _af = _af * jax.random.uniform(jax.random.fold_in(_gk, 3), (8192, 8192), jnp.float32, 0.05, 1)
        adj = _af
        return (x, adj)
    x, adj = _rec_inputs()

    def _L0_gnn_setup():
        import jax, jax.numpy as jnp
        import numpy as np
        N, E, D = (4096, 4096, 128)
        key = jax.random.key(seed)
        k1, k2 = jax.random.split(key)
        X = jax.random.normal(k1, (N, D), dtype=jnp.float32)
        H = jax.random.uniform(k2, (N, E), dtype=jnp.float32)
        return {'X': X, 'H': H}
    _L0_gnn_all = _L0_gnn_setup()
    _L0_gnn_in = {k: v for k, v in _L0_gnn_all.items() if k in ()}
    del _L0_gnn_all
    return {'x': x, 'adj': adj}

def reference(x, adj):
    import jax
    import jax.numpy as jnp

    def _L0_gnn_ref(X, H):
        import jax, jax.numpy as jnp
        import numpy as np
        N, E, D = (4096, 4096, 128)
        msg = jnp.matmul(H.T, X)
        inv_deg = 1.0 / H.sum(axis=0)
        inv_deg = jnp.where(jnp.isinf(inv_deg), 0.0, inv_deg)
        return msg * inv_deg[:, None]
    h = jnp.maximum(_layernorm(x, axis=-1), 0.0)
    x = x + _L0_gnn_ref(h, adj)
    return x

_drawn_inputs = setup_inputs


def setup_inputs(seed=0):
    import zlib

    import numpy as np

    out = dict(_drawn_inputs(seed))
    spreads = {}
    factors = {}
    for name, (base, spread) in spreads.items():
        noise = np.random.default_rng([zlib.crc32(name.encode()), seed]).standard_normal(out[name].shape)
        drawn = base * np.exp(spread * noise) if base else spread * noise
        out[name] = jnp.asarray(drawn.astype(out[name].dtype))
    for name, factor in factors.items():
        out[name] = (out[name] * factor).astype(out[name].dtype)
    return out
```

```python
from contextlib import ExitStack

import numpy as np

import concourse.bass as bass
from concourse import mybir

ALU = mybir.AluOpType
ACT = mybir.ActivationFunctionType
F32 = mybir.dt.float32
F32R = mybir.dt.float32r

P = 128
EPS = 1e-5
FLT_MAX = float(np.finfo(np.float32).max)

BANKS = 8
BANK = 512
RING = 4


def build_gnn_kernel(nc: bass.Bass, x: bass.AP, adj: bass.AP, out: bass.AP):
    N, D = x.shape
    TILES = N // P
    GROUP_COLS = 2048
    GROUPS = N // GROUP_COLS
    BLOCKS = GROUP_COLS // P
    SUM_W = D + 2
    PER_BANK = BANK // SUM_W
    GROUP_BANKS = -(-BLOCKS // PER_BANK)
    HALF_BANKS = GROUP_BANKS // 2
    HALVES = 2
    H_W = 2 * D + 2
    CHUNK = 4
    ITERS = TILES // RING
    assert D == P and CHUNK == RING and GROUP_BANKS < BANKS and GROUP_BANKS == HALVES * HALF_BANKS

    adj_tiles = adj.rearrange("(t p) e -> p t e", p=P)
    x_tiles = x.rearrange("(t p) d -> p t d", p=P)
    out_tiles = out.rearrange("(t p) d -> p t d", p=P)

    def bank_of(g, b):
        return (GROUP_BANKS * g + b) % BANKS

    def half_blocks(half):
        lo = half * HALF_BANKS * PER_BANK
        return lo, min(lo + HALF_BANKS * PER_BANK, BLOCKS)

    with ExitStack() as ctx:
        def sb(name, shape, dt=F32):
            return ctx.enter_context(nc.sbuf_tensor(name, shape, dt))

        def sem(name):
            return ctx.enter_context(nc.semaphore(name))

        adj_raw = sb("adj_raw", [P, RING, GROUP_COLS])
        adj_hi = sb("adj_hi", [P, RING, GROUP_COLS], F32R)
        adj_lo = sb("adj_lo", [P, RING, GROUP_COLS], F32R)
        x_sb = sb("x_sb", [P, TILES, D])
        h_sb = sb("h_sb", [P, TILES, H_W], F32R)
        x_norm = sb("x_norm", [P, CHUNK, D])
        row_stats = sb("row_stats", [P, CHUNK, 6])
        moments = sb("moments", [P, CHUNK, 2])
        eps = sb("eps", [P, CHUNK])
        minus_one = sb("minus_one", [P, CHUNK])
        minus_half = sb("minus_half", [P, CHUNK])
        var_eps = sb("var_eps", [P, CHUNK])
        rstd = sb("rstd", [P, CHUNK])
        neg_mean = sb("neg_mean", [P, CHUNK])
        shift = sb("shift", [P, CHUNK])
        HALF_BLOCKS = HALF_BANKS * PER_BANK
        inv_deg = sb("inv_deg", [P, HALF_BLOCKS])
        inv_finite = sb("inv_finite", [P, HALF_BLOCKS])
        inv_clamped = sb("inv_clamped", [P, HALF_BLOCKS])
        inv_used = sb("inv_used", [P, HALF_BLOCKS])
        sums = ctx.enter_context(nc.psum_tensor("sums", [P, BANKS, BANK], F32))

        adj_landed = [sem(f"adj_landed{k}") for k in range(RING)]
        x_first_landed = sem("x_first_landed")
        x_second_landed = sem("x_second_landed")
        x_rest_landed = sem("x_rest_landed")
        hi_ready = sem("hi_ready")
        lo_ready = sem("lo_ready")
        multiplied = sem("multiplied")
        half_summed = sem("half_summed")
        banks_free = sem("banks_free")
        ones_set = sem("ones_set")
        constants_set = sem("constants_set")
        stats_ready = sem("stats_ready")
        moments_ready = sem("moments_ready")
        var_ready = sem("var_ready")
        rstd_ready = sem("rstd_ready")
        shift_ready = sem("shift_ready")
        norm_ready = sem("norm_ready")
        h_hi_ready = sem("h_hi_ready")
        h_ready = sem("h_ready")
        inv_step = sem("inv_step")
        stored = sem("stored")

        block = ctx.enter_context(nc.Block())

        def unit(g, it, k):
            return g * TILES + RING * it + k

        @block.sync
        def _(sp):
            def load_adj(g, it, k):
                sp.dma_start(adj_raw[:, k, :],
                             adj_tiles[:, RING * it + k, g * GROUP_COLS:(g + 1) * GROUP_COLS]
                             ).then_inc(adj_landed[k], 16)

            def iteration(g, it):
                for k in range(RING):
                    sp.wait_ge(lo_ready, unit(g, it, k) - RING + 1)
                    load_adj(g, it, k)

            sp.dma_start(x_sb[:, 0:CHUNK, :], x_tiles[:, 0:CHUNK, :]).then_inc(x_first_landed, 16)
            for k in range(RING):
                load_adj(0, 0, k)
                if k == 1:
                    sp.dma_start(x_sb[:, CHUNK:2 * CHUNK, :],
                                 x_tiles[:, CHUNK:2 * CHUNK, :]).then_inc(x_second_landed, 16)
            sp.dma_start(x_sb[:, 2 * CHUNK:, :], x_tiles[:, 2 * CHUNK:, :]).then_inc(x_rest_landed, 16)
            with sp.Fori(1, ITERS) as it:
                iteration(0, it)
            for g in range(1, GROUPS):
                with sp.Fori(0, ITERS) as it:
                    iteration(g, it)
            for half in range(HALVES):
                b0, b1 = half_blocks(half)
                sp.wait_ge(banks_free, HALVES * (GROUPS - 1) + half + 1)
                t0 = (GROUPS - 1) * BLOCKS
                sp.dma_start(out_tiles[:, t0 + b0:t0 + b1, :],
                             x_sb[:, t0 + b0:t0 + b1, :]).then_inc(stored, 16)
            sp.wait_ge(stored, 16 * (GROUPS - 1 + HALVES))

        @block.gpsimd
        def _(pool):
            def chunk_scale(c):
                pool.wait_ge(moments_ready, c + 1)
                nc.gpsimd.tensor_tensor(var_eps[:, :], moments[:, :, 1], eps[:, :],
                                        ALU.add).then_inc(var_ready, 1)
                nc.gpsimd.tensor_tensor(neg_mean[:, :], moments[:, :, 0], minus_one[:, :],
                                        ALU.mult).then_inc(var_ready, 1)
                pool.wait_ge(var_ready, 2 * c + 2)
                if not isinstance(c, int) or c > 0:
                    pool.wait_ge(norm_ready, c)
                nc.gpsimd.tensor_tensor(rstd[:, :], var_eps[:, :], minus_half[:, :],
                                        ALU.pow).then_inc(rstd_ready, 1)
                pool.wait_ge(rstd_ready, c + 1)
                nc.gpsimd.tensor_tensor(shift[:, :], neg_mean[:, :], rstd[:, :],
                                        ALU.mult).then_inc(shift_ready, 1)

            nc.gpsimd.memset(eps[:, :], EPS).then_inc(constants_set, 1)
            nc.gpsimd.memset(minus_one[:, :], -1.0).then_inc(constants_set, 1)
            nc.gpsimd.memset(minus_half[:, :], -0.5).then_inc(constants_set, 1)
            pool.wait_ge(constants_set, 3)
            chunk_scale(0)
            with pool.Fori(1, ITERS) as c:
                chunk_scale(c)

        @block.scalar
        def _(act):
            def normalise(c):
                act.wait_ge(shift_ready, c + 1)
                if not isinstance(c, int) or c > 0:
                    act.wait_ge(h_ready, c)
                for k in range(CHUNK):
                    last = nc.scalar.activation(x_norm[:, k, :], x_sb[:, CHUNK * c + k, :], ACT.Identity,
                                                bias=shift[:, k:k + 1], scale=rstd[:, k:k + 1])
                last.then_inc(norm_ready, 1)
                act.wait_ge(norm_ready, c + 1)
                nc.scalar.activation(h_sb[:, bass.ds(CHUNK * c, CHUNK), 0:D], x_norm[:, :, :],
                                     ACT.Relu).then_inc(h_hi_ready, 1)

            def round_adj(g, it, k):
                u = unit(g, it, k)
                act.wait_ge(adj_landed[k], 16 * (g * ITERS + it + 1))
                if g > 0 or not isinstance(it, int) or it > 0:
                    act.wait_ge(multiplied, u - RING + 1)
                nc.scalar.activation(adj_hi[:, k, :], adj_raw[:, k, :], ACT.Copy).then_inc(hi_ready, 1)

            def iteration(g, it, make_h):
                for k in range(RING):
                    round_adj(g, it, k)
                    if k == 2 and make_h:
                        normalise(it + 1)

            normalise(0)
            iteration(0, 0, True)
            with act.Fori(1, ITERS - 1) as it:
                iteration(0, it, True)
            iteration(0, ITERS - 1, False)
            for g in range(1, GROUPS):
                iteration(g, 0, False)
                act.wait_ge(banks_free, HALVES * g)
                act.dma_start(out_tiles[:, (g - 1) * BLOCKS:g * BLOCKS, :],
                              x_sb[:, (g - 1) * BLOCKS:g * BLOCKS, :]).then_inc(stored, 16)
                with act.Fori(1, ITERS) as it:
                    iteration(g, it, False)

        @block.vector
        def _(dve):
            def chunk_stats(c):
                if not isinstance(c, int) or c > 0:
                    dve.wait_ge(var_ready, 2 * c)
                for k in range(CHUNK):
                    last = nc.vector.bn_stats(row_stats[:, k, :], x_sb[:, CHUNK * c + k, :])
                last.then_inc(stats_ready, 1)

            def chunk_moments(c):
                for k in range(CHUNK):
                    last = nc.vector.bn_aggr(moments[:, k, :], row_stats[:, k, :])
                last.then_inc(moments_ready, 1)

            def chunk_h_lo(c):
                dve.wait_ge(h_hi_ready, c + 1)
                tiles = bass.ds(CHUNK * c, CHUNK)
                nc.vector.scalar_tensor_tensor(
                    out=h_sb[:, tiles, D + 2:H_W], in0=x_norm[:, :, :], scalar=0.0,
                    in1=h_sb[:, tiles, 0:D].bitcast(F32), op0=ALU.max, op1=ALU.subtract
                ).then_inc(h_ready, 1)

            def split_adj(g, it, k):
                u = unit(g, it, k)
                dve.wait_ge(hi_ready, u + 1)
                if g > 0 or not isinstance(it, int) or it > 0:
                    dve.wait_ge(multiplied, u - RING + 1)
                nc.vector.tensor_tensor(adj_lo[:, k, :], adj_raw[:, k, :], adj_hi[:, k, :].bitcast(F32),
                                        ALU.subtract).then_inc(lo_ready, 1)

            steps = [0]

            def finish_half(g, half):
                b0, b1 = half_blocks(half)
                n = b1 - b0
                if half == 0:
                    dve.wait_ge(half_summed, g + 1)
                else:
                    dve.wait_ge(multiplied, (g + 1) * TILES)
                for b in range(HALF_BANKS):
                    blocks = min(PER_BANK, n - b * PER_BANK)
                    bank = sums[:, bank_of(g, half * HALF_BANKS + b), 0:blocks * SUM_W]
                    degrees = bank.rearrange("p (j w) -> p j w", w=SUM_W)[:, :, D]
                    last = nc.vector.reciprocal(inv_deg[:, b * PER_BANK:b * PER_BANK + blocks], degrees)
                last.then_inc(inv_step, 1)
                dve.wait_ge(inv_step, steps[0] + 1)
                nc.vector.tensor_scalar(inv_clamped[:, 0:n], inv_deg[:, 0:n], FLT_MAX, -FLT_MAX,
                                        ALU.min, ALU.max).then_inc(inv_step, 1)
                dve.wait_ge(inv_step, steps[0] + 2)
                nc.vector.tensor_tensor(inv_finite[:, 0:n], inv_deg[:, 0:n], inv_clamped[:, 0:n],
                                        ALU.is_equal).then_inc(inv_step, 1)
                dve.wait_ge(inv_step, steps[0] + 3)
                nc.vector.tensor_tensor(inv_used[:, 0:n], inv_clamped[:, 0:n], inv_finite[:, 0:n],
                                        ALU.mult).then_inc(inv_step, 1)
                dve.wait_ge(inv_step, steps[0] + 4)
                steps[0] += 4
                for j in range(n):
                    slot = (j % PER_BANK) * SUM_W
                    rows = g * BLOCKS + b0 + j
                    last = nc.vector.scalar_tensor_tensor(
                        out=x_sb[:, rows, :],
                        in0=sums[:, bank_of(g, half * HALF_BANKS + j // PER_BANK), slot:slot + D],
                        scalar=inv_used[:, j:j + 1], in1=x_sb[:, rows, :], op0=ALU.mult, op1=ALU.add)
                last.then_inc(banks_free, 1)

            def iteration(g, it, make_h):
                for k in range(RING):
                    if make_h and k == 1:
                        dve.wait_ge(stats_ready, it + 2)
                    split_adj(g, it, k)
                    if make_h and k == 0:
                        if isinstance(it, int):
                            dve.wait_ge(x_second_landed, 16)
                        chunk_stats(it + 1)
                    if make_h and k == 1:
                        chunk_moments(it + 1)
                    if make_h and k == 3:
                        chunk_h_lo(it + 1)
                    if k == 2 and isinstance(it, int) and it == 0 and g > 0:
                        finish_half(g - 1, 0)
                        finish_half(g - 1, 1)

            nc.vector.memset(h_sb[:, :, D:D + 1].bitcast(F32), 1.0)
            nc.vector.memset(h_sb[:, :, D + 1:D + 2].bitcast(F32), 0.0).then_inc(ones_set, 1)
            dve.wait_ge(x_first_landed, 16)
            chunk_stats(0)
            dve.wait_ge(stats_ready, 1)
            chunk_moments(0)
            chunk_h_lo(0)
            iteration(0, 0, True)
            dve.wait_ge(x_rest_landed, 16)
            with dve.Fori(1, ITERS - 1) as it:
                iteration(0, it, True)
            iteration(0, ITERS - 1, False)
            for g in range(1, GROUPS):
                iteration(g, 0, False)
                with dve.Fori(1, ITERS) as it:
                    iteration(g, it, False)
            finish_half(GROUPS - 1, 0)
            finish_half(GROUPS - 1, 1)

        @block.tensor
        def _(pe):
            def multiply(g, it, k, first, last):
                u = unit(g, it, k)
                t = RING * it + k
                h_hi_1 = h_sb[:, t, 0:D + 2]
                h_lo = h_sb[:, t, D + 2:H_W]
                pe.wait_ge(hi_ready, u + 1)
                for j in range(BLOCKS):
                    b = j // PER_BANK
                    if first and j % PER_BANK == 0:
                        before = GROUP_BANKS * g + b - BANKS
                        if before >= 0:
                            pe.wait_ge(banks_free, before // HALF_BANKS + 1)
                    bank, slot = bank_of(g, b), (j % PER_BANK) * SUM_W
                    w = adj_hi[:, k, j * P:(j + 1) * P]
                    nc.tensor.matmul(sums[:, bank, slot:slot + SUM_W], w, h_hi_1,
                                     start=first and j % PER_BANK == 0, stop=False, skip_group_check=True)
                    nc.tensor.matmul(sums[:, bank, slot:slot + D], w, h_lo,
                                     start=False, stop=False, skip_group_check=True)
                pe.wait_ge(lo_ready, u + 1)
                for j in range(BLOCKS):
                    bank, slot = bank_of(g, j // PER_BANK), (j % PER_BANK) * SUM_W
                    mm = nc.tensor.matmul(sums[:, bank, slot:slot + SUM_W], adj_lo[:, k, j * P:(j + 1) * P],
                                          h_hi_1, start=False, stop=last, skip_group_check=True)
                    if last and j == half_blocks(0)[1] - 1:
                        mm.then_inc(half_summed, 1)
                mm.then_inc(multiplied, 1)

            def iteration(g, it, first=False, last=False):
                if g == 0:
                    pe.wait_ge(h_ready, it + 1)
                for k in range(RING):
                    multiply(g, it, k, first and k == 0, last and k == RING - 1)

            pe.wait_ge(ones_set, 1)
            for g in range(GROUPS):
                iteration(g, 0, first=True)
                with pe.Fori(1, ITERS - 1) as it:
                    iteration(g, it)
                iteration(g, ITERS - 1, last=True)


_INS = ["x", "adj"]
_OUTS = [((8192, 128), "float32")]


def kernel(**inputs):
    import numpy as _np
    import concourse.bacc as _bacc
    from concourse import mybir as _mybir
    from concourse.bass_utils import run_bass_kernel_spmd as _run

    nc = _bacc.Bacc("TRN2", target_bir_lowering=False, num_devices=1)
    arrays, args = {}, []
    for name in _INS:
        a = _np.ascontiguousarray(inputs[name])
        arrays[f"in_{name}_dram"] = a
        args.append(nc.dram_tensor(f"in_{name}_dram", a.shape, _mybir.dt.from_np(a.dtype), kind="ExternalInput").ap())
    for i, (shape, dtype) in enumerate(_OUTS):
        dt = _mybir.dt.from_np(_np.dtype(dtype))
        args.append(nc.dram_tensor(f"out_{i}_dram", shape, dt, kind="ExternalOutput").ap())
    build_gnn_kernel(nc, *args)
    r = _run(nc, [arrays], core_ids=[0])
    return r.results[0]["out_0_dram"]
```

```python
from contextlib import ExitStack

import numpy as np

import concourse.bass as bass
from concourse import mybir

ALU = mybir.AluOpType
ACT = mybir.ActivationFunctionType
F32 = mybir.dt.float32
F32R = mybir.dt.float32r

P = 128
EPS = 1e-5
FLT_MAX = float(np.finfo(np.float32).max)

BANKS = 8
BANK = 512
RAW = 6
RING = 3


def build_gnn_kernel(nc: bass.Bass, x: bass.AP, adj: bass.AP, out: bass.AP):
    N, D = x.shape
    TILES = N // P
    GROUP_COLS = 2048
    GROUPS = N // GROUP_COLS
    BLOCKS = GROUP_COLS // P
    SPLIT_BLOCKS = 10
    SPLIT_COLS = SPLIT_BLOCKS * P
    WHOLE_BLOCKS = BLOCKS - SPLIT_BLOCKS
    SUM_W = D + 1
    PER_BANK = BANK // SUM_W
    SPLIT_BANKS = -(-SPLIT_COLS // BANK)
    WHOLE_BANKS = -(-WHOLE_BLOCKS // PER_BANK)
    WHOLE_BANK0 = 2 * SPLIT_BANKS
    HEAD = TILES % RAW
    ITERS = TILES // RAW
    assert D == P and RAW % RING == 0 and 0 < HEAD <= RAW
    assert WHOLE_BANK0 + WHOLE_BANKS <= BANKS and WHOLE_BLOCKS == WHOLE_BANKS * PER_BANK
    pieces = [(c, min(BANK, SPLIT_COLS - c)) for c in range(0, SPLIT_COLS, BANK)]
    DEG0 = SPLIT_COLS - (SPLIT_BANKS - 1) * BANK
    assert DEG0 + SPLIT_BLOCKS <= BANK

    adj_tiles = adj.rearrange("(t p) e -> p t e", p=P)
    x_tiles = x.rearrange("(t p) d -> p t d", p=P)
    out_tiles = out.rearrange("(t p) d -> p t d", p=P)

    with ExitStack() as ctx:
        def sb(name, shape, dt=F32):
            return ctx.enter_context(nc.sbuf_tensor(name, shape, dt))

        def sem(name):
            return ctx.enter_context(nc.semaphore(name))

        adj_raw = sb("adj_raw", [P, RAW, GROUP_COLS])
        adj_hi = sb("adj_hi", [P, RING, SPLIT_COLS], F32R)
        adj_lo = sb("adj_lo", [P, RING, SPLIT_COLS], F32R)
        x_sb = sb("x_sb", [P, TILES, D])
        h_one = sb("h_one", [P, TILES, SUM_W])
        h_lo = sb("h_lo", [P, TILES, D])
        h_rounded = sb("h_rounded", [P, RAW, D], F32R)
        h_fixed = sb("h_fixed", [P, RING, 2, D], F32R)
        deg_part = sb("deg_part", [P, 2, SPLIT_COLS])
        split_sums = sb("split_sums", [P, SPLIT_COLS + SPLIT_BLOCKS])
        whole_sums = sb("whole_sums", [P, WHOLE_BLOCKS, SUM_W])
        identity = sb("identity", [P, P])
        one = sb("one", [P, 1])
        row_stats = sb("row_stats", [P, RAW, 6])
        moments = sb("moments", [P, RAW, 2])
        eps = sb("eps", [P, RAW])
        minus_one = sb("minus_one", [P, RAW])
        minus_half = sb("minus_half", [P, RAW])
        var_eps = sb("var_eps", [P, RAW])
        rstd = sb("rstd", [P, RAW])
        neg_mean = sb("neg_mean", [P, RAW])
        shift = sb("shift", [P, RAW])
        inv_deg = sb("inv_deg", [P, BLOCKS])
        inv_clamped = sb("inv_clamped", [P, BLOCKS])
        inv_finite = sb("inv_finite", [P, BLOCKS])
        inv_used = sb("inv_used", [P, BLOCKS])
        sums = ctx.enter_context(nc.psum_tensor("sums", [P, BANKS, BANK], F32))

        adj_landed = [sem(f"adj_landed{k}") for k in range(RAW)]
        x_first_landed = sem("x_first_landed")
        x_second_landed = sem("x_second_landed")
        x_rest_landed = sem("x_rest_landed")
        hi_ready = sem("hi_ready")
        lo_ready = sem("lo_ready")
        deg_added = sem("deg_added")
        multiplied = sem("multiplied")
        whole_final = sem("whole_final")
        split_final = sem("split_final")
        whole_copied = sem("whole_copied")
        split_copied = sem("split_copied")
        turned = sem("turned")
        finished = sem("finished")
        whole_finished = sem("whole_finished")
        constants_set = sem("constants_set")
        ones_set = sem("ones_set")
        stats_ready = sem("stats_ready")
        moments_ready = sem("moments_ready")
        var_ready = sem("var_ready")
        rstd_ready = sem("rstd_ready")
        shift_ready = sem("shift_ready")
        relu_ready = sem("relu_ready")
        rounded_ready = sem("rounded_ready")
        h_ready = sem("h_ready")
        inv_step = sem("inv_step")
        stored = sem("stored")

        block = ctx.enter_context(nc.Block())

        def tile_of(i, k):
            return k if i is None else HEAD + RAW * i + k

        def unit(g, i, k):
            return g * TILES + tile_of(i, k)

        def slot(g, i, k, slots):
            return (g * TILES + (k if i is None else HEAD + k)) % slots

        def uses(g, i, k):
            if i is None:
                return (g * TILES + k) // RAW + 1
            return (g * TILES + HEAD + k) // RAW + i + 1

        def wait_back(eng, semaphore, g, i, k, back):
            if g > 0 or not (i is None or isinstance(i, int)) or tile_of(i, k) >= back:
                eng.wait_ge(semaphore, unit(g, i, k) - back + 1)

        def chunk_tiles(i):
            return (0, HEAD) if i is None else (HEAD + RAW * i, RAW)

        def chunk_no(i):
            return 0 if i is None else i + 1

        def next_chunk(i):
            return 0 if i is None else i + 1

        def split_bank(g, b):
            return SPLIT_BANKS * (g % 2) + b

        @block.sync
        def _(sp):
            def load_adj(g, i, k):
                s = slot(g, i, k, RAW)
                sp.dma_start(adj_raw[:, s, :],
                             adj_tiles[:, tile_of(i, k), g * GROUP_COLS:(g + 1) * GROUP_COLS]
                             ).then_inc(adj_landed[s], 16)

            def reload(g, i, count):
                for k in range(count):
                    wait_back(sp, multiplied, g, i, k, RAW)
                    wait_back(sp, deg_added, g, i, k, RAW)
                    load_adj(g, i, k)

            sp.dma_start(x_sb[:, 0:HEAD, :], x_tiles[:, 0:HEAD, :]).then_inc(x_first_landed, 16)
            load_adj(0, None, 0)
            load_adj(0, None, 1)
            sp.dma_start(x_sb[:, HEAD:HEAD + RAW, :],
                         x_tiles[:, HEAD:HEAD + RAW, :]).then_inc(x_second_landed, 16)
            for k in range(2, HEAD):
                load_adj(0, None, k)
            reload(0, 0, RAW - HEAD)
            sp.dma_start(x_sb[:, HEAD + RAW:, :], x_tiles[:, HEAD + RAW:, :]).then_inc(x_rest_landed, 16)
            for k in range(RAW - HEAD, RAW):
                wait_back(sp, multiplied, 0, 0, k, RAW)
                wait_back(sp, deg_added, 0, 0, k, RAW)
                load_adj(0, 0, k)
            with sp.Fori(1, ITERS) as i:
                reload(0, i, RAW)
            for g in range(1, GROUPS):
                reload(g, None, HEAD)
                with sp.Fori(0, ITERS) as i:
                    reload(g, i, RAW)
            t0 = (GROUPS - 1) * BLOCKS
            sp.wait_ge(whole_finished, GROUPS)
            sp.dma_start(out_tiles[:, t0 + SPLIT_BLOCKS:, :],
                         x_sb[:, t0 + SPLIT_BLOCKS:, :]).then_inc(stored, 16)
            sp.wait_ge(finished, GROUPS)
            sp.dma_start(out_tiles[:, t0:t0 + SPLIT_BLOCKS, :],
                         x_sb[:, t0:t0 + SPLIT_BLOCKS, :]).then_inc(stored, 16)
            sp.wait_ge(stored, 16 * (GROUPS + 1))

        @block.gpsimd
        def _(pool):
            def chunk_scale(c, n):
                pool.wait_ge(moments_ready, c + 1)
                nc.gpsimd.tensor_tensor(var_eps[:, 0:n], moments[:, 0:n, 1], eps[:, 0:n],
                                        ALU.add).then_inc(var_ready, 1)
                nc.gpsimd.tensor_tensor(neg_mean[:, 0:n], moments[:, 0:n, 0], minus_one[:, 0:n],
                                        ALU.mult).then_inc(var_ready, 1)
                pool.wait_ge(var_ready, 2 * c + 2)
                if not isinstance(c, int) or c > 0:
                    pool.wait_ge(relu_ready, c)
                nc.gpsimd.tensor_tensor(rstd[:, 0:n], var_eps[:, 0:n], minus_half[:, 0:n],
                                        ALU.pow).then_inc(rstd_ready, 1)
                pool.wait_ge(rstd_ready, c + 1)
                nc.gpsimd.tensor_tensor(shift[:, 0:n], neg_mean[:, 0:n], rstd[:, 0:n],
                                        ALU.mult).then_inc(shift_ready, 1)

            nc.gpsimd.memset(eps[:, :], EPS).then_inc(constants_set, 1)
            nc.gpsimd.memset(minus_one[:, :], -1.0).then_inc(constants_set, 1)
            nc.gpsimd.memset(minus_half[:, :], -0.5).then_inc(constants_set, 1)
            nc.gpsimd.memset(identity[:, :], 0.0).then_inc(constants_set, 1)
            nc.gpsimd.memset(one[:, :], 1.0).then_inc(ones_set, 1)
            pool.wait_ge(constants_set, 4)
            nc.gpsimd.affine_select(out=identity[:, :], in_=identity[:, :], compare_op=ALU.not_equal,
                                    fill=1.0, base=0, pattern=[[-1, P]],
                                    channel_multiplier=1).then_inc(ones_set, 1)
            chunk_scale(0, HEAD)
            with pool.Fori(1, ITERS + 1) as c:
                chunk_scale(c, RAW)

        @block.scalar
        def _(act):
            def normalise(i):
                t0, n = chunk_tiles(i)
                c = chunk_no(i)
                act.wait_ge(shift_ready, c + 1)
                if not isinstance(c, int) or c > 0:
                    act.wait_ge(h_ready, c)
                for k in range(n):
                    last = nc.scalar.activation(h_one[:, t0 + k, 0:D], x_sb[:, t0 + k, :], ACT.Relu,
                                                bias=shift[:, k:k + 1], scale=rstd[:, k:k + 1])
                last.then_inc(relu_ready, 1)

            def round_h(i):
                t0, n = chunk_tiles(i)
                nc.scalar.activation(h_rounded[:, 0:n, :], h_one[:, bass.ds(t0, n), 0:D],
                                     ACT.Copy).then_inc(rounded_ready, 1)

            def round_adj(g, i, k):
                s = slot(g, i, k, RING)
                if g == 0 and k == 0:
                    act.wait_ge(h_ready, chunk_no(i) + 1)
                act.wait_ge(adj_landed[slot(g, i, k, RAW)], 16 * uses(g, i, k))
                wait_back(act, multiplied, g, i, k, RING)
                nc.scalar.activation(adj_hi[:, s, :], adj_raw[:, slot(g, i, k, RAW), 0:SPLIT_COLS],
                                     ACT.Copy).then_inc(hi_ready, 1)
                t = tile_of(i, k)
                nc.scalar.activation(h_fixed[:, s, 0, :], h_one[:, t, 0:D], ACT.Copy)
                nc.scalar.activation(h_fixed[:, s, 1, :], h_lo[:, t, :], ACT.Copy).then_inc(hi_ready, 1)

            def copy_whole(g):
                act.wait_ge(whole_final, g + 1)
                if g > 0:
                    act.wait_ge(finished, g)
                for b in range(WHOLE_BANKS):
                    last = nc.scalar.activation(
                        whole_sums[:, b * PER_BANK:(b + 1) * PER_BANK, :],
                        sums[:, WHOLE_BANK0 + b, 0:PER_BANK * SUM_W].rearrange("p (j w) -> p j w", w=SUM_W),
                        ACT.Copy)
                last.then_inc(whole_copied, 1)

            def copy_split(g):
                act.wait_ge(split_final, g + 1)
                for b, (c, w) in enumerate(pieces):
                    w += SPLIT_BLOCKS if b == SPLIT_BANKS - 1 else 0
                    last = nc.scalar.activation(split_sums[:, c:c + w], sums[:, split_bank(g, b), 0:w],
                                                ACT.Copy)
                last.then_inc(split_copied, 1)

            def iteration(g, i, count, make_h):
                for k in range(count):
                    if k == 3 and make_h:
                        act.wait_ge(relu_ready, chunk_no(next_chunk(i)) + 1)
                    round_adj(g, i, k)
                    if k == 2 and make_h:
                        normalise(next_chunk(i))
                    if k == 3 and make_h:
                        round_h(next_chunk(i))

            normalise(None)
            act.wait_ge(relu_ready, 1)
            round_h(None)
            iteration(0, None, HEAD, True)
            with act.Fori(0, ITERS - 1) as i:
                iteration(0, i, RAW, True)
            iteration(0, ITERS - 1, RAW, False)
            for g in range(1, GROUPS):
                for k in range(HEAD):
                    round_adj(g, None, k)
                    if k == 1:
                        copy_whole(g - 1)
                    if k == 2:
                        copy_split(g - 1)
                iteration(g, 0, RAW, False)
                act.wait_ge(finished, g)
                act.dma_start(out_tiles[:, (g - 1) * BLOCKS:g * BLOCKS, :],
                              x_sb[:, (g - 1) * BLOCKS:g * BLOCKS, :]).then_inc(stored, 16)
                with act.Fori(1, ITERS) as i:
                    iteration(g, i, RAW, False)
            copy_whole(GROUPS - 1)
            copy_split(GROUPS - 1)

        @block.vector
        def _(dve):
            def chunk_stats(i):
                t0, n = chunk_tiles(i)
                c = chunk_no(i)
                if not isinstance(c, int) or c > 0:
                    dve.wait_ge(var_ready, 2 * c)
                for k in range(n):
                    last = nc.vector.bn_stats(row_stats[:, k, :], x_sb[:, t0 + k, :])
                last.then_inc(stats_ready, 1)

            def chunk_moments(i):
                n = chunk_tiles(i)[1]
                for k in range(n):
                    last = nc.vector.bn_aggr(moments[:, k, :], row_stats[:, k, :])
                last.then_inc(moments_ready, 1)

            def chunk_h_lo(i):
                t0, n = chunk_tiles(i)
                dve.wait_ge(rounded_ready, chunk_no(i) + 1)
                nc.vector.tensor_tensor(h_lo[:, bass.ds(t0, n), :], h_one[:, bass.ds(t0, n), 0:D],
                                        h_rounded[:, 0:n, :].bitcast(F32), ALU.subtract).then_inc(h_ready, 1)

            def split_adj(g, i, k):
                s, raw = slot(g, i, k, RING), slot(g, i, k, RAW)
                dve.wait_ge(hi_ready, 2 * unit(g, i, k) + 1)
                wait_back(dve, multiplied, g, i, k, RING)
                nc.vector.tensor_tensor(adj_lo[:, s, :], adj_raw[:, raw, 0:SPLIT_COLS],
                                        adj_hi[:, s, :].bitcast(F32), ALU.subtract).then_inc(lo_ready, 1)

            def add_degrees(g, i, k):
                part = deg_part[:, g % 2, :]
                adj_cols = adj_raw[:, slot(g, i, k, RAW), 0:SPLIT_COLS]
                if i is None and k == 0:
                    if g >= 2:
                        dve.wait_ge(split_final, g - 1)
                    nc.vector.tensor_copy(part, adj_cols).then_inc(deg_added, 1)
                else:
                    wait_back(dve, deg_added, g, i, k, 1)
                    nc.vector.tensor_tensor(part, part, adj_cols, ALU.add).then_inc(deg_added, 1)

            steps = [0]

            def step(instruction):
                steps[0] += 1
                instruction.then_inc(inv_step, 1)
                dve.wait_ge(inv_step, steps[0])

            def inverse(degrees, b0, n):
                used = slice(b0, b0 + n)
                step(nc.vector.reciprocal(inv_deg[:, used], degrees))
                step(nc.vector.tensor_scalar(inv_clamped[:, used], inv_deg[:, used], FLT_MAX, -FLT_MAX,
                                             ALU.min, ALU.max))
                step(nc.vector.tensor_tensor(inv_finite[:, used], inv_deg[:, used], inv_clamped[:, used],
                                             ALU.is_equal))
                step(nc.vector.tensor_tensor(inv_used[:, used], inv_clamped[:, used], inv_finite[:, used],
                                             ALU.mult))

            def finish_block(g, b, total):
                rows = g * BLOCKS + b
                return nc.vector.scalar_tensor_tensor(
                    out=x_sb[:, rows, :], in0=total, scalar=inv_used[:, b:b + 1], in1=x_sb[:, rows, :],
                    op0=ALU.mult, op1=ALU.add)

            def finish_whole(g):
                dve.wait_ge(whole_copied, g + 1)
                inverse(whole_sums[:, :, D], SPLIT_BLOCKS, WHOLE_BLOCKS)
                for b in range(WHOLE_BLOCKS):
                    last = finish_block(g, SPLIT_BLOCKS + b, whole_sums[:, b, 0:D])
                last.then_inc(whole_finished, 1)

            def invert_split(g):
                dve.wait_ge(split_copied, g + 1)
                inverse(split_sums[:, SPLIT_COLS:SPLIT_COLS + SPLIT_BLOCKS], 0, SPLIT_BLOCKS)

            def finish_split(g, b0, b1):
                dve.wait_ge(turned, g + 1)
                per_bank = BANK // P
                for b in range(b0, b1):
                    c = (b % per_bank) * P
                    last = finish_block(g, b, sums[:, split_bank(g, b // per_bank), c:c + P])
                if b1 == SPLIT_BLOCKS:
                    last.then_inc(finished, 1)

            def finish_during(g, k):
                if k == 0:
                    finish_whole(g - 1)
                elif k == 1:
                    invert_split(g - 1)
                    finish_split(g - 1, 0, 2)
                else:
                    finish_split(g - 1, 2 * k - 2, 2 * k)

            def iteration(g, i, count, make_h, finish=False):
                for k in range(count):
                    if make_h and k == 1:
                        dve.wait_ge(stats_ready, chunk_no(next_chunk(i)) + 1)
                    split_adj(g, i, k)
                    if make_h and k == 1:
                        chunk_moments(next_chunk(i))
                    add_degrees(g, i, k)
                    if make_h and k == 0:
                        chunk_stats(next_chunk(i))
                    if make_h and k == min(4, count - 1):
                        chunk_h_lo(next_chunk(i))
                    if finish:
                        finish_during(g, k)

            nc.vector.memset(h_one[:, :, D:D + 1], 1.0).then_inc(ones_set, 1)
            dve.wait_ge(x_first_landed, 16)
            chunk_stats(None)
            dve.wait_ge(stats_ready, 1)
            chunk_moments(None)
            chunk_h_lo(None)
            dve.wait_ge(x_second_landed, 16)
            iteration(0, None, HEAD, True)
            dve.wait_ge(x_rest_landed, 16)
            with dve.Fori(0, ITERS - 1) as i:
                iteration(0, i, RAW, True)
            iteration(0, ITERS - 1, RAW, False)
            for g in range(1, GROUPS):
                iteration(g, None, HEAD, False)
                iteration(g, 0, RAW, False, finish=True)
                with dve.Fori(1, ITERS) as i:
                    iteration(g, i, RAW, False)
            finish_whole(GROUPS - 1)
            invert_split(GROUPS - 1)
            finish_split(GROUPS - 1, 0, SPLIT_BLOCKS)

        @block.tensor
        def _(pe):
            def multiply_whole(g, i, k, first, last):
                if first and g > 0:
                    pe.wait_ge(whole_copied, g)
                raw, t = slot(g, i, k, RAW), tile_of(i, k)
                for j in range(WHOLE_BLOCKS):
                    c = SPLIT_COLS + j * P
                    w = (j % PER_BANK) * SUM_W
                    mm = nc.tensor.matmul(sums[:, WHOLE_BANK0 + j // PER_BANK, w:w + SUM_W],
                                          adj_raw[:, raw, c:c + P], h_one[:, t, :],
                                          start=first and j % PER_BANK == 0, stop=last,
                                          skip_group_check=True)
                if last:
                    mm.then_inc(whole_final, 1)
                return mm

            def multiply_split(g, i, k, first, last):
                if first and g >= 2:
                    pe.wait_ge(finished, g - 1)
                s = slot(g, i, k, RING)
                h_hi, h_low = h_fixed[:, s, 0, :], h_fixed[:, s, 1, :]
                for weights, start in ((h_hi, first), (h_low, False)):
                    for b, (c, w) in enumerate(pieces):
                        nc.tensor.matmul(sums[:, split_bank(g, b), 0:w], weights, adj_hi[:, s, c:c + w],
                                         start=start, stop=False, skip_group_check=True)
                pe.wait_ge(lo_ready, unit(g, i, k) + 1)
                for b, (c, w) in enumerate(pieces):
                    mm = nc.tensor.matmul(sums[:, split_bank(g, b), 0:w], h_hi, adj_lo[:, s, c:c + w],
                                          start=False, stop=last, skip_group_check=True)
                return mm

            def multiply(g, i, k, first=False, last=False):
                pe.wait_ge(hi_ready, 2 * unit(g, i, k) + 2)
                if first:
                    multiply_split(g, i, k, first, last)
                    mm = multiply_whole(g, i, k, first, last)
                else:
                    multiply_whole(g, i, k, first, last)
                    mm = multiply_split(g, i, k, first, last)
                mm.then_inc(multiplied, 1)

            def sum_degrees(g):
                pe.wait_ge(deg_added, (g + 1) * TILES)
                for j in range(SPLIT_BLOCKS):
                    mm = nc.tensor.matmul(sums[:, split_bank(g, SPLIT_BANKS - 1), DEG0 + j:DEG0 + j + 1],
                                          deg_part[:, g % 2, j * P:(j + 1) * P], one[:, :],
                                          start=True, stop=True, skip_group_check=True)
                mm.then_inc(split_final, 1)

            def turn_split(g):
                pe.wait_ge(split_copied, g + 1)
                per_bank = BANK // P
                for j in range(SPLIT_BLOCKS):
                    c = (j % per_bank) * P
                    mm = nc.tensor.transpose(sums[:, split_bank(g, j // per_bank), c:c + P],
                                             split_sums[:, j * P:(j + 1) * P], identity[:, :])
                mm.then_inc(turned, 1)

            pe.wait_ge(ones_set, 3)
            for g in range(GROUPS):
                for k in range(HEAD):
                    multiply(g, None, k, first=(k == 0))
                    if g > 0 and k == 2:
                        turn_split(g - 1)
                with pe.Fori(0, ITERS - 1) as i:
                    for k in range(RAW):
                        multiply(g, i, k)
                for k in range(RAW):
                    multiply(g, ITERS - 1, k, last=(k == RAW - 1))
                sum_degrees(g)
            turn_split(GROUPS - 1)


_INS = ["x", "adj"]
_OUTS = [((8192, 128), "float32")]


def kernel(**inputs):
    import numpy as _np
    import concourse.bacc as _bacc
    from concourse import mybir as _mybir
    from concourse.bass_utils import run_bass_kernel_spmd as _run

    nc = _bacc.Bacc("TRN2", target_bir_lowering=False, num_devices=1)
    arrays, args = {}, []
    for name in _INS:
        a = _np.ascontiguousarray(inputs[name])
        arrays[f"in_{name}_dram"] = a
        args.append(nc.dram_tensor(f"in_{name}_dram", a.shape, _mybir.dt.from_np(a.dtype), kind="ExternalInput").ap())
    for i, (shape, dtype) in enumerate(_OUTS):
        dt = _mybir.dt.from_np(_np.dtype(dtype))
        args.append(nc.dram_tensor(f"out_{i}_dram", shape, dt, kind="ExternalOutput").ap())
    build_gnn_kernel(nc, *args)
    r = _run(nc, [arrays], core_ids=[0])
    return r.results[0]["out_0_dram"]
```

```python
from contextlib import ExitStack

import numpy as np

import concourse.bass as bass
from concourse import mybir

ALU = mybir.AluOpType
ACT = mybir.ActivationFunctionType
F32 = mybir.dt.float32
F32R = mybir.dt.float32r

P = 128
EPS = 1e-5
FLT_MAX = float(np.finfo(np.float32).max)

BANKS = 8
BANK = 512
RAW = 6
RING = 3


def build_gnn_kernel(nc: bass.Bass, x: bass.AP, adj: bass.AP, out: bass.AP):
    N, D = x.shape
    TILES = N // P
    GROUP_COLS = 2048
    GROUPS = N // GROUP_COLS
    BLOCKS = GROUP_COLS // P
    SPLIT_BLOCKS = 10
    SPLIT_COLS = SPLIT_BLOCKS * P
    WHOLE_BLOCKS = BLOCKS - SPLIT_BLOCKS
    SUM_W = D + 1
    PER_BANK = BANK // SUM_W
    SPLIT_BANKS = -(-SPLIT_COLS // BANK)
    WHOLE_BANKS = -(-WHOLE_BLOCKS // PER_BANK)
    WHOLE_BANK0 = 2 * SPLIT_BANKS
    HEAD = TILES % RAW
    ITERS = TILES // RAW
    assert D == P and RAW % RING == 0 and 0 < HEAD <= RAW
    assert WHOLE_BANK0 + WHOLE_BANKS <= BANKS and WHOLE_BLOCKS == WHOLE_BANKS * PER_BANK
    pieces = [(c, min(BANK, SPLIT_COLS - c)) for c in range(0, SPLIT_COLS, BANK)]
    DEG0 = pieces[-1][1]
    PER_PIECE = BANK // P
    x_parts = [0, HEAD, HEAD + RAW, HEAD + 3 * RAW, HEAD + 5 * RAW, HEAD + 7 * RAW, TILES]
    stretches = [(1, 3), (3, 5), (5, ITERS)]
    assert DEG0 + SPLIT_BLOCKS <= BANK and PER_PIECE * (SPLIT_BANKS - 1) < SPLIT_BLOCKS

    adj_tiles = adj.rearrange("(t p) e -> p t e", p=P)
    x_tiles = x.rearrange("(t p) d -> p t d", p=P)
    out_tiles = out.rearrange("(t p) d -> p t d", p=P)

    with ExitStack() as ctx:
        def sb(name, shape, dt=F32):
            return ctx.enter_context(nc.sbuf_tensor(name, shape, dt))

        def sem(name):
            return ctx.enter_context(nc.semaphore(name))

        adj_raw = sb("adj_raw", [P, RAW, GROUP_COLS])
        adj_hi = sb("adj_hi", [P, RING, SPLIT_COLS], F32R)
        adj_lo = sb("adj_lo", [P, RING, SPLIT_COLS], F32R)
        x_sb = sb("x_sb", [P, TILES, D])
        h_all = sb("h_all", [P, TILES, 2 * SUM_W])
        h_parts = h_all[:, :, :].rearrange("p t (a w) -> p t a w", w=SUM_W)
        h_rounded = sb("h_rounded", [P, RAW, D], F32R)
        h_fixed = sb("h_fixed", [P, RING, 2, D], F32R)
        deg_part = sb("deg_part", [P, 2, SPLIT_COLS])
        split_sums = sb("split_sums", [P, SPLIT_COLS])
        whole_sums = sb("whole_sums", [P, WHOLE_BANKS, PER_BANK * SUM_W])
        identity = sb("identity", [P, P])
        one = sb("one", [P, 1])
        head_stats = sb("head_stats", [P, HEAD, 6])
        head_moments = sb("head_moments", [P, HEAD, 2])
        row_sum = sb("row_sum", [P, RAW])
        square_sum = sb("square_sum", [P, RAW])
        minus_share = sb("minus_share", [P, RAW])
        share = sb("share", [P, RAW])
        eps = sb("eps", [P, RAW])
        minus_half = sb("minus_half", [P, RAW])
        neg_mean = sb("neg_mean", [P, RAW])
        var = sb("var", [P, RAW])
        var_eps = sb("var_eps", [P, RAW])
        rstd = sb("rstd", [P, RAW])
        shift = sb("shift", [P, RAW])
        inv_deg = sb("inv_deg", [P, BLOCKS])
        inv_clamped = sb("inv_clamped", [P, BLOCKS])
        inv_finite = sb("inv_finite", [P, BLOCKS])
        inv_used = sb("inv_used", [P, BLOCKS])
        sums = ctx.enter_context(nc.psum_tensor("sums", [P, BANKS, BANK], F32))

        adj_landed = [sem(f"adj_landed{k}") for k in range(RAW)]
        x_landed = [sem(f"x_landed{n}") for n in range(len(x_parts) - 1)]
        hi_ready = sem("hi_ready")
        lo_ready = sem("lo_ready")
        deg_added = sem("deg_added")
        multiplied = sem("multiplied")
        whole_final = sem("whole_final")
        degrees_final = sem("degrees_final")
        split_final = sem("split_final")
        whole_copied = sem("whole_copied")
        split_copied = sem("split_copied")
        turned = sem("turned")
        finished = sem("finished")
        whole_finished = sem("whole_finished")
        bank_finished = sem("bank_finished")
        constants_set = sem("constants_set")
        ones_set = sem("ones_set")
        head_step = sem("head_step")
        head_var_ready = sem("head_var_ready")
        sums_ready = sem("sums_ready")
        mean_ready = sem("mean_ready")
        squares_ready = sem("squares_ready")
        var_ready = sem("var_ready")
        rstd_ready = sem("rstd_ready")
        shift_ready = sem("shift_ready")
        relu_ready = sem("relu_ready")
        rounded_ready = sem("rounded_ready")
        h_ready = sem("h_ready")
        inv_step = sem("inv_step")
        stored = sem("stored")

        block = ctx.enter_context(nc.Block())

        def tile_of(i, k):
            return k if i is None else HEAD + RAW * i + k

        def unit(g, i, k):
            return g * TILES + tile_of(i, k)

        def slot(g, i, k, slots):
            return (g * TILES + (k if i is None else HEAD + k)) % slots

        def uses(g, i, k):
            if i is None:
                return (g * TILES + k) // RAW + 1
            return (g * TILES + HEAD + k) // RAW + i + 1

        def wait_back(eng, semaphore, g, i, k, back):
            if g > 0 or not (i is None or isinstance(i, int)) or tile_of(i, k) >= back:
                eng.wait_ge(semaphore, unit(g, i, k) - back + 1)

        def chunk_tiles(i):
            return (0, HEAD) if i is None else (HEAD + RAW * i, RAW)

        def chunk_after(i, n=1):
            return n - 1 if i is None else i + n

        def wait_chunk(eng, semaphore, i):
            eng.wait_ge(semaphore, 1 if i is None else i + 2)

        def wait_scale(eng, semaphore, i):
            eng.wait_ge(semaphore, i + 1)

        def split_bank(g, b):
            return SPLIT_BANKS * (g % 2) + b

        def whole_bank_sums(b=slice(0, WHOLE_BANKS)):
            return sums[:, WHOLE_BANK0 + b.start:WHOLE_BANK0 + b.stop, 0:PER_BANK * SUM_W]

        def degree_columns(g):
            return sums[:, split_bank(g if g < GROUPS - 1 else g + 1, SPLIT_BANKS - 1),
                        DEG0:DEG0 + SPLIT_BLOCKS]

        @block.sync
        def _(sp):
            def load_adj(g, i, k):
                s = slot(g, i, k, RAW)
                sp.dma_start(adj_raw[:, s, :],
                             adj_tiles[:, tile_of(i, k), g * GROUP_COLS:(g + 1) * GROUP_COLS]
                             ).then_inc(adj_landed[s], 16)

            def reload(g, i, k0, k1):
                for k in range(k0, k1):
                    wait_back(sp, multiplied, g, i, k, RAW)
                    wait_back(sp, deg_added, g, i, k, RAW)
                    load_adj(g, i, k)

            def load_x(n):
                rows = slice(x_parts[n], x_parts[n + 1])
                sp.dma_start(x_sb[:, rows, :], x_tiles[:, rows, :]).then_inc(x_landed[n], 16)

            load_x(0)
            reload(0, None, 0, 1)
            load_x(1)
            reload(0, None, 1, 3)
            reload(0, None, 3, HEAD)
            load_x(2)
            reload(0, 0, 0, RAW)
            for n, (i0, i1) in enumerate(stretches):
                load_x(3 + n)
                with sp.Fori(i0, i1) as i:
                    reload(0, i, 0, RAW)
            for g in range(1, GROUPS):
                reload(g, None, 0, HEAD)
                reload(g, 0, 0, RAW)
                reload(g, 1, 0, RAW)
                sp.wait_ge(finished, g)
                sp.dma_start(out_tiles[:, (g - 1) * BLOCKS:g * BLOCKS, :],
                             x_sb[:, (g - 1) * BLOCKS:g * BLOCKS, :]).then_inc(stored, 16)
                with sp.Fori(2, ITERS) as i:
                    reload(g, i, 0, RAW)
            t0 = (GROUPS - 1) * BLOCKS
            sp.wait_ge(whole_finished, GROUPS)
            sp.dma_start(out_tiles[:, t0 + SPLIT_BLOCKS:, :],
                         x_sb[:, t0 + SPLIT_BLOCKS:, :]).then_inc(stored, 16)
            for b, (c, w) in enumerate(pieces):
                if b < SPLIT_BANKS - 1:
                    sp.wait_ge(bank_finished, b + 1)
                else:
                    sp.wait_ge(finished, GROUPS)
                rows = slice(t0 + c // P, t0 + (c + w) // P)
                sp.dma_start(out_tiles[:, rows, :], x_sb[:, rows, :]).then_inc(stored, 16)
            sp.wait_ge(stored, 16 * (GROUPS + SPLIT_BANKS))

        @block.gpsimd
        def _(pool):
            def chunk_scale(i):
                n = chunk_tiles(i)[1]
                wait_scale(pool, sums_ready, i)
                nc.gpsimd.tensor_tensor(neg_mean[:, 0:n], row_sum[:, 0:n], minus_share[:, 0:n],
                                        ALU.mult).then_inc(mean_ready, 1)
                wait_scale(pool, squares_ready, i)
                nc.gpsimd.tensor_tensor(var[:, 0:n], square_sum[:, 0:n], share[:, 0:n],
                                        ALU.mult).then_inc(var_ready, 1)
                pool.wait_ge(var_ready, 2 * i + 1)
                nc.gpsimd.tensor_tensor(var_eps[:, 0:n], var[:, 0:n], eps[:, 0:n],
                                        ALU.add).then_inc(var_ready, 1)
                pool.wait_ge(var_ready, 2 * i + 2)
                pool.wait_ge(relu_ready, i + 1)
                nc.gpsimd.tensor_tensor(rstd[:, 0:n], var_eps[:, 0:n], minus_half[:, 0:n],
                                        ALU.pow).then_inc(rstd_ready, 1)
                wait_chunk(pool, rstd_ready, i)
                nc.gpsimd.tensor_tensor(shift[:, 0:n], neg_mean[:, 0:n], rstd[:, 0:n],
                                        ALU.mult).then_inc(shift_ready, 1)

            for constant, value in ((minus_share, -1.0 / D), (share, 1.0 / D), (eps, EPS),
                                    (minus_half, -0.5), (identity, 0.0)):
                nc.gpsimd.memset(constant[:, :], value).then_inc(constants_set, 1)
            nc.gpsimd.memset(one[:, :], 1.0).then_inc(ones_set, 1)
            pool.wait_ge(constants_set, 5)
            nc.gpsimd.affine_select(out=identity[:, :], in_=identity[:, :], compare_op=ALU.not_equal,
                                    fill=1.0, base=0, pattern=[[-1, P]],
                                    channel_multiplier=1).then_inc(ones_set, 1)
            pool.wait_ge(head_var_ready, 1)
            nc.gpsimd.tensor_tensor(rstd[:, 0:HEAD], var_eps[:, 0:HEAD], minus_half[:, 0:HEAD],
                                    ALU.pow).then_inc(rstd_ready, 1)
            pool.wait_ge(rstd_ready, 1)
            with pool.Fori(0, ITERS) as i:
                chunk_scale(i)

        @block.scalar
        def _(act):
            def sum_rows(i):
                t0, n = chunk_tiles(i)
                for k in range(n):
                    last = nc.scalar.activation(h_all[:, t0 + k, 0:D], x_sb[:, t0 + k, :], ACT.Copy,
                                                accum_out=row_sum[:, k:k + 1])
                last.then_inc(sums_ready, 1)

            def sum_squares(i):
                t0, n = chunk_tiles(i)
                for k in range(n):
                    last = nc.scalar.activation(h_all[:, t0 + k, 0:D], x_sb[:, t0 + k, :], ACT.Square,
                                                bias=neg_mean[:, k:k + 1],
                                                accum_out=square_sum[:, k:k + 1])
                last.then_inc(squares_ready, 1)

            def normalise(i):
                t0, n = chunk_tiles(i)
                for k in range(n):
                    last = nc.scalar.activation(h_all[:, t0 + k, 0:D], x_sb[:, t0 + k, :], ACT.Relu,
                                                bias=shift[:, k:k + 1], scale=rstd[:, k:k + 1])
                last.then_inc(relu_ready, 1)

            def round_h(i):
                t0, n = chunk_tiles(i)
                nc.scalar.activation(h_rounded[:, 0:n, :], h_all[:, bass.ds(t0, n), 0:D],
                                     ACT.Copy).then_inc(rounded_ready, 1)

            def round_adj(g, i, k):
                s = slot(g, i, k, RING)
                in_loop = not (i is None or isinstance(i, int))
                if g == 0 and k == 0 and in_loop:
                    wait_chunk(act, h_ready, i)
                act.wait_ge(adj_landed[slot(g, i, k, RAW)], 16 * uses(g, i, k))
                wait_back(act, multiplied, g, i, k, RING)
                nc.scalar.activation(adj_hi[:, s, :], adj_raw[:, slot(g, i, k, RAW), 0:SPLIT_COLS],
                                     ACT.Copy).then_inc(hi_ready, 1)
                if g == 0 and k == 0 and not in_loop:
                    wait_chunk(act, h_ready, i)
                nc.scalar.activation(h_fixed[:, s, :, :], h_parts[:, tile_of(i, k), :, 0:D],
                                     ACT.Copy).then_inc(hi_ready, 1)

            def copy_whole(g):
                act.wait_ge(whole_final, g + 1)
                if g > 0:
                    act.wait_ge(whole_finished, g)
                for b in range(WHOLE_BANKS):
                    last = nc.scalar.activation(whole_sums[:, b:b + 1, :],
                                                whole_bank_sums(slice(b, b + 1)), ACT.Copy)
                last.then_inc(whole_copied, 1)

            def copy_split(g):
                for b, (c, w) in enumerate(pieces):
                    if b < SPLIT_BANKS - 1:
                        act.wait_ge(split_final, (SPLIT_BANKS - 1) * g + b + 1)
                    else:
                        act.wait_ge(multiplied, (g + 1) * TILES)
                    nc.scalar.activation(split_sums[:, c:c + w], sums[:, split_bank(g, b), 0:w],
                                         ACT.Copy).then_inc(split_copied, 1)

            def iteration(g, i, next_h=False, later_h=False):
                after, later = chunk_after(i), chunk_after(i, 2)
                for k in range(RAW):
                    if next_h and k == 1:
                        wait_scale(act, shift_ready, after)
                    if next_h and k == 2:
                        wait_chunk(act, relu_ready, after)
                    if later_h and k == 5:
                        wait_scale(act, mean_ready, later)
                    round_adj(g, i, k)
                    if next_h and k == 1:
                        normalise(after)
                    if next_h and k == 2:
                        round_h(after)
                    if later_h and k == 4:
                        sum_rows(later)
                    if later_h and k == 5:
                        sum_squares(later)

            act.wait_ge(relu_ready, 1)
            round_h(None)
            round_adj(0, None, 0)
            act.wait_ge(x_landed[1], 16)
            sum_rows(0)
            round_adj(0, None, 1)
            act.wait_ge(mean_ready, 1)
            sum_squares(0)
            round_adj(0, None, 2)
            round_adj(0, None, 3)
            act.wait_ge(shift_ready, 1)
            normalise(0)
            act.wait_ge(relu_ready, 2)
            round_h(0)
            round_adj(0, 0, 0)
            act.wait_ge(x_landed[2], 16)
            sum_rows(1)
            round_adj(0, 0, 1)
            act.wait_ge(mean_ready, 2)
            sum_squares(1)
            round_adj(0, 0, 2)
            act.wait_ge(shift_ready, 2)
            round_adj(0, 0, 3)
            normalise(1)
            act.wait_ge(relu_ready, 3)
            round_adj(0, 0, 4)
            round_h(1)
            sum_rows(2)
            act.wait_ge(mean_ready, 3)
            round_adj(0, 0, 5)
            sum_squares(2)
            assert HEAD == 4 and RAW == 6
            for n, (i0, i1) in enumerate(stretches):
                act.wait_ge(x_landed[3 + n], 16)
                with act.Fori(i0, min(i1, ITERS - 2)) as i:
                    iteration(0, i, True, True)
            iteration(0, ITERS - 2, True)
            iteration(0, ITERS - 1)
            for g in range(1, GROUPS):
                for k in range(HEAD):
                    round_adj(g, None, k)
                    if k == 1:
                        copy_whole(g - 1)
                    if k == 2:
                        copy_split(g - 1)
                with act.Fori(0, ITERS) as i:
                    iteration(g, i)
            copy_split(GROUPS - 1)

        @block.vector
        def _(dve):
            def head_relu():
                dve.wait_ge(x_landed[0], 16)
                for k in range(HEAD):
                    nc.vector.bn_stats(head_stats[:, k, :], x_sb[:, k, :]).then_inc(head_step, 1)
                for k in range(HEAD):
                    dve.wait_ge(head_step, k + 1)
                    nc.vector.bn_aggr(head_moments[:, k, :], head_stats[:, k, :]).then_inc(head_step, 1)
                dve.wait_ge(head_step, 2 * HEAD)
                nc.vector.tensor_scalar(var_eps[:, 0:HEAD], head_moments[:, :, 1], EPS, None,
                                        ALU.add).then_inc(head_var_ready, 1)
                for k in range(HEAD):
                    nc.vector.tensor_scalar(h_all[:, k, 0:D], x_sb[:, k, :], head_moments[:, k, 0:1],
                                            None, ALU.subtract).then_inc(head_step, 1)
                dve.wait_ge(head_step, 3 * HEAD)
                dve.wait_ge(rstd_ready, 1)
                for k in range(HEAD):
                    last = nc.vector.tensor_scalar(h_all[:, k, 0:D], h_all[:, k, 0:D],
                                                   rstd[:, k:k + 1], 0.0, ALU.mult, ALU.max)
                last.then_inc(relu_ready, 1)

            def chunk_h_lo(i):
                t0, n = chunk_tiles(i)
                wait_chunk(dve, rounded_ready, i)
                nc.vector.tensor_tensor(h_all[:, bass.ds(t0, n), SUM_W:SUM_W + D],
                                        h_all[:, bass.ds(t0, n), 0:D],
                                        h_rounded[:, 0:n, :].bitcast(F32), ALU.subtract).then_inc(h_ready, 1)

            def split_adj(g, i, k):
                s, raw = slot(g, i, k, RING), slot(g, i, k, RAW)
                dve.wait_ge(hi_ready, 2 * unit(g, i, k) + 1)
                wait_back(dve, multiplied, g, i, k, RING)
                nc.vector.tensor_tensor(adj_lo[:, s, :], adj_raw[:, raw, 0:SPLIT_COLS],
                                        adj_hi[:, s, :].bitcast(F32), ALU.subtract).then_inc(lo_ready, 1)

            def add_degrees(g, i, k):
                part = deg_part[:, g % 2, :]
                adj_cols = adj_raw[:, slot(g, i, k, RAW), 0:SPLIT_COLS]
                if i is None and k == 0:
                    if g >= 2:
                        dve.wait_ge(degrees_final, g - 1)
                    nc.vector.tensor_copy(part, adj_cols).then_inc(deg_added, 1)
                else:
                    wait_back(dve, deg_added, g, i, k, 1)
                    nc.vector.tensor_tensor(part, part, adj_cols, ALU.add).then_inc(deg_added, 1)

            steps = [0]

            def step(instruction):
                steps[0] += 1
                instruction.then_inc(inv_step, 1)
                dve.wait_ge(inv_step, steps[0])

            def inverse(degrees, b0, banks, per_bank):
                def used(values):
                    return values[:, b0:b0 + banks * per_bank].rearrange("p (b j) -> p b j", j=per_bank)

                step(nc.vector.reciprocal(used(inv_deg), degrees))
                step(nc.vector.tensor_scalar(used(inv_clamped), used(inv_deg), FLT_MAX, -FLT_MAX,
                                             ALU.min, ALU.max))
                step(nc.vector.tensor_tensor(used(inv_finite), used(inv_deg), used(inv_clamped),
                                             ALU.is_equal))
                step(nc.vector.tensor_tensor(used(inv_used), used(inv_clamped), used(inv_finite),
                                             ALU.mult))

            def finish_block(g, b, total):
                rows = g * BLOCKS + b
                return nc.vector.scalar_tensor_tensor(
                    out=x_sb[:, rows, :], in0=total, scalar=inv_used[:, b:b + 1], in1=x_sb[:, rows, :],
                    op0=ALU.mult, op1=ALU.add)

            def finish_whole(g, bank_sums):
                whole = bank_sums.rearrange("p b (j w) -> p b j w", w=SUM_W)
                inverse(whole[:, :, :, D], SPLIT_BLOCKS, WHOLE_BANKS, PER_BANK)
                for j in range(WHOLE_BLOCKS):
                    last = finish_block(g, SPLIT_BLOCKS + j, whole[:, j // PER_BANK, j % PER_BANK, 0:D])
                last.then_inc(whole_finished, 1)

            def inverse_split(g):
                inverse(degree_columns(g).rearrange("p (b j) -> p b j", b=1), 0, 1, SPLIT_BLOCKS)

            def finish_split(g, b0, b1):
                for b in range(b0, b1):
                    bank, c = b // PER_PIECE, (b % PER_PIECE) * P
                    if b == b0 or b % PER_PIECE == 0:
                        dve.wait_ge(turned, SPLIT_BANKS * g + bank + 1)
                    last = finish_block(g, b, sums[:, split_bank(g, bank), c:c + P])
                if b1 == SPLIT_BLOCKS:
                    last.then_inc(finished, 1)
                return last

            def finish_during(g, k):
                if k == 0:
                    dve.wait_ge(whole_copied, g)
                    finish_whole(g - 1, whole_sums[:, :, :])
                else:
                    if k == 1:
                        dve.wait_ge(turned, SPLIT_BANKS * g)
                        inverse_split(g - 1)
                    finish_split(g - 1, 2 * k - 2, 2 * k)

            def iteration(g, i, count, h_behind=None, finish=False):
                for k in range(count):
                    split_adj(g, i, k)
                    add_degrees(g, i, k)
                    if k == h_behind:
                        chunk_h_lo(chunk_after(i))
                    if finish:
                        finish_during(g, k)

            nc.vector.memset(h_all[:, :, D:D + 1], 1.0).then_inc(ones_set, 1)
            head_relu()
            chunk_h_lo(None)
            iteration(0, None, HEAD, h_behind=HEAD - 1)
            iteration(0, 0, RAW, h_behind=4)
            with dve.Fori(1, ITERS - 1) as i:
                iteration(0, i, RAW, h_behind=3)
            iteration(0, ITERS - 1, RAW)
            for g in range(1, GROUPS):
                iteration(g, None, HEAD)
                iteration(g, 0, RAW, finish=True)
                with dve.Fori(1, ITERS) as i:
                    iteration(g, i, RAW)
            dve.wait_ge(whole_final, GROUPS)
            finish_whole(GROUPS - 1, whole_bank_sums())
            dve.wait_ge(degrees_final, GROUPS)
            inverse_split(GROUPS - 1)
            for b in range(SPLIT_BANKS - 1):
                finish_split(GROUPS - 1, b * PER_PIECE,
                             (b + 1) * PER_PIECE).then_inc(bank_finished, 1)
            finish_split(GROUPS - 1, (SPLIT_BANKS - 1) * PER_PIECE, SPLIT_BLOCKS)

        @block.tensor
        def _(pe):
            BETWEEN = 3 * SPLIT_BANKS - 1
            WARM_UP = 22

            def nothing(j):
                pass

            def multiply_whole(g, i, k, first, last):
                if first and g > 0:
                    pe.wait_ge(whole_copied, g)
                raw, t = slot(g, i, k, RAW), tile_of(i, k)
                for j in range(WHOLE_BLOCKS):
                    c = SPLIT_COLS + j * P
                    w = (j % PER_BANK) * SUM_W
                    mm = nc.tensor.matmul(sums[:, WHOLE_BANK0 + j // PER_BANK, w:w + SUM_W],
                                          adj_raw[:, raw, c:c + P], h_all[:, t, 0:SUM_W],
                                          start=first and j % PER_BANK == 0, stop=last,
                                          skip_group_check=True)
                return mm

            def multiply_split(g, i, k, first, last, between=nothing):
                if first and g >= 2:
                    pe.wait_ge(finished, g - 1)
                s = slot(g, i, k, RING)
                h_hi, h_low = h_fixed[:, s, 0, :], h_fixed[:, s, 1, :]
                products = ((h_hi, adj_hi), (h_low, adj_hi), (h_hi, adj_lo))
                if last:
                    order = [(p, b) for b in range(SPLIT_BANKS) for p in range(3)]
                else:
                    order = [(p, b) for p in range(3) for b in range(SPLIT_BANKS)]
                for j, (p, b) in enumerate(order):
                    (weights, moving), (c, w) = products[p], pieces[b]
                    if j == order.index((2, 0)):
                        pe.wait_ge(lo_ready, unit(g, i, k) + 1)
                    mm = nc.tensor.matmul(sums[:, split_bank(g, b), 0:w], weights, moving[:, s, c:c + w],
                                          start=first and p == 0, stop=last and p == 2,
                                          skip_group_check=True)
                    if last and p == 2 and b < SPLIT_BANKS - 1:
                        mm.then_inc(split_final, 1)
                    if j < BETWEEN:
                        between(j)
                return mm

            def multiply(g, i, k, first=False, last=False, between=nothing):
                if g == 0 and k == 0:
                    wait_chunk(pe, relu_ready, i)
                pe.wait_ge(hi_ready, 2 * unit(g, i, k) + 1)
                if first and g > 0:
                    pe.wait_ge(hi_ready, 2 * unit(g, i, k) + 2)
                    mm = multiply_split(g, i, k, first, last, between)
                    mm = multiply_whole(g, i, k, first, last)
                else:
                    mm = multiply_whole(g, i, k, first, last)
                    if last:
                        mm.then_inc(whole_final, 1)
                    pe.wait_ge(hi_ready, 2 * unit(g, i, k) + 2)
                    mm = multiply_split(g, i, k, first, last, between)
                mm.then_inc(multiplied, 1)

            def sum_degrees(g, j):
                mm = nc.tensor.matmul(degree_columns(g)[:, j:j + 1],
                                      deg_part[:, g % 2, j * P:(j + 1) * P], one[:, :],
                                      start=True, stop=True, skip_group_check=True)
                if j == SPLIT_BLOCKS - 1:
                    mm.then_inc(degrees_final, 1)

            def turn_block(g, j):
                b, c = j // PER_PIECE, (j % PER_PIECE) * P
                if c == 0:
                    pe.wait_ge(split_copied, SPLIT_BANKS * g + b + 1)
                mm = nc.tensor.transpose(sums[:, split_bank(g, b), c:c + P],
                                         split_sums[:, j * P:(j + 1) * P], identity[:, :])
                if c + P == pieces[b][1]:
                    mm.then_inc(turned, 1)

            def between_last(j):
                if 2 * j < SPLIT_BLOCKS:
                    for d in range(2 * j, min(2 * j + 2, SPLIT_BLOCKS)):
                        sum_degrees(GROUPS - 1, d)
                if j == 3 * (SPLIT_BANKS - 1) - 1:
                    for d in range(PER_PIECE):
                        turn_block(GROUPS - 1, d)

            pe.wait_ge(ones_set, 3)
            for _ in range(WARM_UP):
                mm = nc.tensor.matmul(sums[:, split_bank(1, 0), 0:P], identity[:, :], identity[:, :],
                                      start=True, stop=True, skip_group_check=True)
            for g in range(GROUPS):
                for k in range(HEAD):
                    if g > 0 and k == 2:
                        pe.wait_ge(deg_added, g * TILES)
                        pe.wait_ge(split_copied, SPLIT_BANKS * g)
                        multiply(g, None, k, between=lambda j: sum_degrees(g - 1, j))
                        for j in range(BETWEEN, SPLIT_BLOCKS):
                            sum_degrees(g - 1, j)
                    elif g > 0 and k == 3:
                        multiply(g, None, k, between=lambda j: turn_block(g - 1, j))
                        for j in range(BETWEEN, SPLIT_BLOCKS):
                            turn_block(g - 1, j)
                    else:
                        multiply(g, None, k, first=(k == 0))
                with pe.Fori(0, ITERS - 1) as i:
                    for k in range(RAW):
                        multiply(g, i, k)
                for k in range(RAW - 1):
                    multiply(g, ITERS - 1, k)
                if g < GROUPS - 1:
                    multiply(g, ITERS - 1, RAW - 1, last=True)
            g = GROUPS - 1
            pe.wait_ge(deg_added, GROUPS * TILES)
            pe.wait_ge(finished, g)
            multiply(g, ITERS - 1, RAW - 1, last=True, between=between_last)
            for j in range(PER_PIECE, SPLIT_BLOCKS):
                turn_block(g, j)


_INS = ["x", "adj"]
_OUTS = [((8192, 128), "float32")]


def kernel(**inputs):
    import numpy as _np
    import concourse.bacc as _bacc
    from concourse import mybir as _mybir
    from concourse.bass_utils import run_bass_kernel_spmd as _run

    nc = _bacc.Bacc("TRN2", target_bir_lowering=False, num_devices=1)
    arrays, args = {}, []
    for name in _INS:
        a = _np.ascontiguousarray(inputs[name])
        arrays[f"in_{name}_dram"] = a
        args.append(nc.dram_tensor(f"in_{name}_dram", a.shape, _mybir.dt.from_np(a.dtype), kind="ExternalInput").ap())
    for i, (shape, dtype) in enumerate(_OUTS):
        dt = _mybir.dt.from_np(_np.dtype(dtype))
        args.append(nc.dram_tensor(f"out_{i}_dram", shape, dt, kind="ExternalOutput").ap())
    build_gnn_kernel(nc, *args)
    r = _run(nc, [arrays], core_ids=[0])
    return r.results[0]["out_0_dram"]
```
